# Optimizing a Trainium2 kernel written in Bass

```python
import numpy as np
import jax
import jax.numpy as jnp

def _softmax(x, axis=-1):
    return jax.nn.softmax(x, axis=axis)

def _gelu(x):
    return jax.nn.gelu(x, approximate=True)

def _silu(x):
    return jax.nn.silu(x)

def _sigmoid(x):
    return jax.nn.sigmoid(x)

def _layernorm(x, axis=-1, eps=1e-05):
    m = jnp.mean(x, axis=axis, keepdims=True)
    v = jnp.var(x, axis=axis, keepdims=True)
    return (x - m) / jnp.sqrt(v + eps)

def _scatter_add(tgt, idx, src, axis=0):
    return tgt.at[idx].add(src)

def _segment_sum(src, seg, n):
    return jax.ops.segment_sum(src, seg, n)
kernel_name = 'mk_adaln_ffn_d1_seqx_r8_f2ea4c'

def setup_inputs(seed: int=0):
    np.random.seed(seed)
    _w = jnp.asarray

    def _rec_inputs():
        import jax
        import jax.numpy as jnp
        _rk = jax.random.key(seed)
        x = -7.109e-05 + 0.9999 * jax.random.normal(jax.random.fold_in(_rk, 1), (32, 32, 256), jnp.float32)
        _lenS = 32 - jax.random.randint(jax.random.fold_in(_rk, 7), (32,), 0, max(1, 32 // 4) + 1, jnp.int32)
        _lenS2 = 32 - jax.random.randint(jax.random.fold_in(_rk, 8), (32,), 0, max(1, 32 // 4) + 1, jnp.int32)
        itok_B_0_6 = jax.random.randint(jax.random.fold_in(_rk, 11), (32,), 0, 7, jnp.int32)
        return (x, itok_B_0_6)
    x, itok_B_0_6 = _rec_inputs()

    def _L0_cond_setup():
        import jax, jax.numpy as jnp
        import numpy as np
        B, T, D_IN, D_OUT = (16, 256, 256, 256)
        N_ADAPTERS, RANK = (8, 16)
        key = jax.random.key(seed)
        k_x, k_w, k_a, k_b, k_s, k_idx = jax.random.split(key, 6)
        x = jax.random.normal(k_x, (B, T, D_IN), dtype=jnp.float32)
        W = jax.random.normal(k_w, (D_OUT, D_IN), dtype=jnp.float32) * (1.0 / np.sqrt(D_IN))
        A = jax.random.normal(k_a, (N_ADAPTERS, RANK, D_IN), dtype=jnp.float32) * 0.02
        Bm = jax.random.normal(k_b, (N_ADAPTERS, D_OUT, RANK), dtype=jnp.float32) * 0.02
        scalings = jnp.ones((N_ADAPTERS,), dtype=jnp.float32)
        adapter_idx = jax.random.randint(k_idx, (B,), 0, N_ADAPTERS, dtype=jnp.int32)
        return {'x': x, 'W': W, 'A': A, 'Bm': Bm, 'scalings': scalings, 'adapter_idx': adapter_idx}
    _L0_cond_all = _L0_cond_setup()
    _L0_cond_in = {k: v for k, v in _L0_cond_all.items() if k in ('W', 'A', 'Bm', 'scalings')}
    del _L0_cond_all

    def _L0_ffn_setup():
        import jax, jax.numpy as jnp
        import numpy as np
        _Q_IN = 128
        _LUT_MIN = -128
        _Q_OUT = 1 << 16
        _TOP_K = 2
        _EXP_LUT = (jnp.exp(jnp.arange(_LUT_MIN, 1, dtype=jnp.float32) / _Q_IN) * _Q_OUT).astype(jnp.int32)

        def softmax_integer(logits):
            li = jnp.round(logits.astype(jnp.float32) * _Q_IN).astype(jnp.int32)
            shifted = jnp.clip(li - li.max(axis=-1, keepdims=True), _LUT_MIN, None)
            exp_vals = _EXP_LUT[shifted - _LUT_MIN]
            exp_sum = jnp.clip(exp_vals.sum(axis=-1, keepdims=True), 1, None)
            return exp_vals.astype(jnp.float32) / exp_sum.astype(jnp.float32)
        key = jax.random.key(seed)
        k0, k1, k2, k3, k4 = jax.random.split(key, 5)
        B, S, H, I, E = (4, 256, 256, 704, 8)
        x = jax.random.normal(k0, (B, S, H), dtype=jnp.float32)
        w_gate = jax.random.normal(k1, (E, H), dtype=jnp.float32) * 0.02
        w1 = jax.random.normal(k2, (E, I, H), dtype=jnp.float32) * 0.02
        w2 = jax.random.normal(k3, (E, H, I), dtype=jnp.float32) * 0.02
        w3 = jax.random.normal(k4, (E, I, H), dtype=jnp.float32) * 0.02
        return {'x': x, 'w_gate': w_gate, 'w1': w1, 'w2': w2, 'w3': w3}
    _L0_ffn_all = _L0_ffn_setup()
    _L0_ffn_in = {k: v for k, v in _L0_ffn_all.items() if k in ('w_gate', 'w1', 'w2', 'w3')}
    del _L0_ffn_all
    return {'x': x, 'itok_B_0_6': itok_B_0_6, 'L0_cond_W': _L0_cond_in['W'], 'L0_cond_A': _L0_cond_in['A'], 'L0_cond_Bm': _L0_cond_in['Bm'], 'L0_cond_scalings': _L0_cond_in['scalings'], 'L0_ffn_w_gate': _L0_ffn_in['w_gate'], 'L0_ffn_w1': _L0_ffn_in['w1'], 'L0_ffn_w2': _L0_ffn_in['w2'], 'L0_ffn_w3': _L0_ffn_in['w3']}

def reference(x, itok_B_0_6, L0_cond_W, L0_cond_A, L0_cond_Bm, L0_cond_scalings, L0_ffn_w_gate, L0_ffn_w1, L0_ffn_w2, L0_ffn_w3):
    import jax
    import jax.numpy as jnp

    def _L0_cond_ref(x, W, A, Bm, scalings, adapter_idx):
        import jax, jax.numpy as jnp
        import numpy as np
        B, T, D_IN, D_OUT = (16, 256, 256, 256)
        N_ADAPTERS, RANK = (8, 16)
        H = jnp.einsum('btd,od->bto', x, W)
        A_b = A[adapter_idx]
        B_b = Bm[adapter_idx]
        s_b = scalings[adapter_idx]
        xa = jnp.einsum('btd,brd->btr', x, A_b)
        delta = jnp.einsum('btr,bor->bto', xa, B_b)
        delta = jax.lax.stop_gradient(delta * s_b[:, None, None])
        return H + delta

    def _L0_ffn_ref(x, w_gate, w1, w2, w3):
        import jax, jax.numpy as jnp
        import numpy as np
        _Q_IN = 128
        _LUT_MIN = -128
        _Q_OUT = 1 << 16
        _TOP_K = 2
        _EXP_LUT = (jnp.exp(jnp.arange(_LUT_MIN, 1, dtype=jnp.float32) / _Q_IN) * _Q_OUT).astype(jnp.int32)

        def softmax_integer(logits):
            li = jnp.round(logits.astype(jnp.float32) * _Q_IN).astype(jnp.int32)
            shifted = jnp.clip(li - li.max(axis=-1, keepdims=True), _LUT_MIN, None)
            exp_vals = _EXP_LUT[shifted - _LUT_MIN]
            exp_sum = jnp.clip(exp_vals.sum(axis=-1, keepdims=True), 1, None)
            return exp_vals.astype(jnp.float32) / exp_sum.astype(jnp.float32)
        orig_shape = x.shape
        H = orig_shape[-1]
        xf = x.reshape(-1, H)
        T = xf.shape[0]
        E = w_gate.shape[0]
        router_logits = xf @ w_gate.T
        routing_weights = softmax_integer(router_logits)
        top_w, top_i = jax.lax.top_k(routing_weights, _TOP_K)
        top_w = top_w / top_w.sum(axis=-1, keepdims=True)
        combine = jnp.zeros((T, E), xf.dtype).at[jnp.arange(T)[:, None], top_i].add(top_w)
        out = jnp.zeros_like(xf)
        for e in range(E):
            h = jax.nn.silu(xf @ w1[e].T) * (xf @ w3[e].T)
            out = out + combine[:, e:e + 1] * (h @ w2[e].T)
        return out.reshape(orig_shape)
    x = x + _L0_ffn_ref(_L0_cond_ref(x, L0_cond_W, L0_cond_A, L0_cond_Bm, L0_cond_scalings, itok_B_0_6), L0_ffn_w_gate, L0_ffn_w1, L0_ffn_w2, L0_ffn_w3)
    return x

_drawn_inputs = setup_inputs


def setup_inputs(seed=0):
    import zlib

    import numpy as np

    out = dict(_drawn_inputs(seed))
    spreads = {'L0_cond_scalings': (1.0, 0.6)}
    factors = {'L0_cond_A': 8.0, 'L0_cond_Bm': 8.0}
    for name, (base, spread) in spreads.items():
        noise = np.random.default_rng([zlib.crc32(name.encode()), seed]).standard_normal(out[name].shape)
        drawn = base * np.exp(spread * noise) if base else spread * noise
        out[name] = jnp.asarray(drawn.astype(out[name].dtype))
    for name, factor in factors.items():
        out[name] = (out[name] * factor).astype(out[name].dtype)
    return out
```

```python
from contextlib import ExitStack

import concourse.bass as bass
from concourse import mybir

P = 128
TOKENS = 1024
DIM = 256
KC = DIM // P
HALF = 512
HALVES = TOKENS // HALF
BATCH, SEQ = 32, 32
ADAPTERS, RANK = 8, 16
EXPERTS = 8
HIDDEN = 704
FULL = HIDDEN // P
TAIL = HIDDEN - FULL * P
TILES = TOKENS // P
PAIRS = EXPERTS // 2

GU_COLS = 2 * HIDDEN
UP_AT = FULL * P
TAILS_AT = 2 * FULL * P
DOWN_AT = KC * GU_COLS
W_COLS = DOWN_AT + FULL * DIM

PK_W = 0
PK_A = PK_W + KC * DIM
PK_B = PK_A + KC * P
PK_G = PK_B + DIM
PK_S = PK_G + KC * EXPERTS
PK_COLS = PK_S + 1

UNITS = 4
PER_UNIT = FULL + 1
ITEMS = UNITS * PER_UNIT
FULLS = UNITS * FULL
DOWNS = ITEMS - 2
LAG = 2
RING = 4

Q_IN = 128.0
LUT_MIN = -128.0
EXP_POLY = [1.2659316303564871e-11, 9.735014572243017e-09, 6.169693278934574e-06,
            0.0031588352285325527, 1.2130615711212158, 310.5437927246094, 39749.59375]
ROUND_SIGNED = 1.5 * 2.0 ** 23
ROUND_POSITIVE = 2.0 ** 23

ALU = mybir.AluOpType
ACT = mybir.ActivationFunctionType
F32 = mybir.dt.float32
F32R = mybir.dt.float32r
I32 = mybir.dt.int32
AX_X = mybir.AxisListType.X


def unit_of(n):
    return n // (2 * PER_UNIT), (n // PER_UNIT) % 2, n % PER_UNIT


def has_down(n):
    par, _, j = unit_of(n)
    return par == 1 or j < FULL


def fulls_through(n):
    return sum(unit_of(m)[2] < FULL for m in range(n + 1))


def downs_through(n):
    return sum(has_down(m) for m in range(n + 1))


def moe_kernel(nc, x_dram, pack_dram, idx_dram, w_dram, wtail_dram, comb_dram, out_dram):
    with ExitStack() as ctx:
        def sb(name, shape, dt=F32):
            return ctx.enter_context(nc.sbuf_tensor(name, shape, dt))

        def ps(name, shape):
            return ctx.enter_context(nc.psum_tensor(name, shape, F32))

        def sem(name):
            return ctx.enter_context(nc.semaphore(name))

        x = sb("x", [P, KC, TOKENS])
        idx = sb("idx", [P, BATCH], I32)
        idx_f = sb("idx_f", [P, BATCH])
        adapter_i = sb("adapter_i", [P, 1], I32)
        adapter_f = sb("adapter_f", [P, 1])
        adapter_mask = sb("adapter_mask", [P, BATCH])
        c_hi = sb("c_hi", [P, KC, TOKENS], F32R)
        c_lo = sb("c_lo", [P, KC, TOKENS], F32R)
        ident = sb("ident", [P, P])
        zeros = sb("zeros", [P, HALF], F32R)
        tie = sb("tie", [P, TILES * EXPERTS])
        rt = sb("rt", [P, 10, TILES * EXPERTS])
        rs = sb("rs", [P, 6, TILES])
        combT = sb("combT", [EXPERTS, TOKENS])
        w_raw = [sb(f"w_raw{i}", [P, W_COLS]) for i in range(2)]
        w_hi = [sb(f"w_hi{i}", [P, W_COLS], F32R) for i in range(2)]
        w_lo = [sb(f"w_lo{i}", [P, W_COLS], F32R) for i in range(2)]
        wt_raw = sb("wt_raw", [P, DIM])
        wt_hi = sb("wt_hi", [P, DIM], F32R)
        wt_lo = sb("wt_lo", [P, DIM], F32R)
        sg = [sb(f"sg{i}", [P, HALF]) for i in range(2)]
        hid = sb("hid", [P, HALF])
        hidc = sb("hidc", [P, HALF])
        h_hi = [sb(f"h_hi{i}", [P, HALF], F32R) for i in range(RING)]
        h_lo = [sb(f"h_lo{i}", [P, HALF], F32R) for i in range(RING)]
        t_hi = [sb(f"t_hi{i}", [P, HALF], F32R) for i in range(HALVES)]
        t_lo = [sb(f"t_lo{i}", [P, HALF], F32R) for i in range(HALVES)]
        with ExitStack() as early:
            def sb_early(name, shape, dt=F32):
                return early.enter_context(nc.sbuf_tensor(name, shape, dt))

            x_hi = sb_early("x_hi", [P, KC, TOKENS], F32R)
            x_lo = sb_early("x_lo", [P, KC, TOKENS], F32R)
            xa = sb_early("xa", [P, TOKENS])
            xa_hi = sb_early("xa_hi", [P, TOKENS], F32R)
            xa_lo = sb_early("xa_lo", [P, TOKENS], F32R)
            pack = sb_early("pack", [P, PK_COLS])
            pk_hi = sb_early("pk_hi", [P, PK_S], F32R)
            pk_lo = sb_early("pk_lo", [P, PK_S], F32R)
        comb = sb("comb", [P, EXPERTS * TOKENS])
        out_sb = sb("out_sb", [P, HALVES, KC, HALF])

        acc = ps("acc", [P, HALVES, KC, HALF])
        gate_ps = [ps(f"gate_ps{i}", [P, HALF]) for i in range(2)]
        up_ps = [ps(f"up_ps{i}", [P, HALF]) for i in range(2)]

        x_in = [sem(f"x_in{h}") for h in range(HALVES)]
        pack_in = sem("pack_in")
        idx_in = sem("idx_in")
        w_in = [sem(f"w_in{i}") for i in range(2)]
        wt_in = sem("wt_in")
        consts_ready = sem("consts_ready")
        pool_step = sem("pool_step")
        pk_hi_ready = sem("pk_hi_ready")
        pk_lo_ready = sem("pk_lo_ready")
        x_hi_ready = sem("x_hi_ready")
        x_lo_ready = sem("x_lo_ready")
        xa_done = sem("xa_done")
        xa_masked = sem("xa_masked")
        xa_hi_ready = sem("xa_hi_ready")
        xa_lo_ready = sem("xa_lo_ready")
        cond_done = sem("cond_done")
        c_hi_ready = sem("c_hi_ready")
        c_lo_ready = sem("c_lo_ready")
        logits_done = sem("logits_done")
        logits_read = sem("logits_read")
        dve_step = sem("dve_step")
        combine_ready = sem("combine_ready")
        combT_done = sem("combT_done")
        combT_copied = sem("combT_copied")
        combT_stored = sem("combT_stored")
        comb_first_in = sem("comb_first_in")
        comb_rest_in = sem("comb_rest_in")
        wgu_split = sem("wgu_split")
        wd_split = sem("wd_split")
        wt_split = sem("wt_split")
        whi_step = sem("whi_step")
        gates_done = sem("gates_done")
        ups_done = sem("ups_done")
        silu_done = sem("silu_done")
        hid_done = sem("hid_done")
        hidc_done = sem("hidc_done")
        h_hi_ready = sem("h_hi_ready")
        h_lo_ready = sem("h_lo_ready")
        downs_done = sem("downs_done")
        out_ready = sem("out_ready")
        out_stored = sem("out_stored")

        def as_f32(ap):
            return ap.bitcast(F32)

        def item_buffers(n, hi, lo):
            par, half, j = unit_of(n)
            if j < FULL:
                return hi[n % RING][:, :], lo[n % RING][:, :], slice(0, P)
            rows = slice(par * TAIL, par * TAIL + TAIL)
            return t_hi[half][rows, :], t_lo[half][rows, :], rows

        block = ctx.enter_context(nc.Block())

        @block.sync
        def _(sp):
            for h in range(HALVES):
                tok = slice(h * HALF, (h + 1) * HALF)
                sp.dma_start(x[:, :, tok], x_dram[:, :, tok]).then_inc(x_in[h], 16)
            for i in range(2):
                sp.dma_start(w_raw[i][:, :], w_dram[i, :, :]).then_inc(w_in[i], 16)
            sp.dma_start(wt_raw[:, :], wtail_dram[0, :, :]).then_inc(wt_in, 16)
            sp.wait_ge(combT_copied, 1)
            sp.dma_start(comb_dram[:, :], combT[:, :]).then_inc(combT_stored, 16)
            sp.wait_ge(combT_stored, 16)
            flat = comb_dram.rearrange("(a e) t -> a (e t)", a=1)
            sp.dma_start(comb[:, 0:TOKENS],
                         flat[:, 0:TOKENS].broadcast_to([P, TOKENS])).then_inc(comb_first_in, 16)
            sp.dma_start(comb[:, TOKENS:],
                         flat[:, TOKENS:].broadcast_to([P, (EXPERTS - 1) * TOKENS])).then_inc(comb_rest_in, 16)
            with sp.Fori(1, PAIRS) as p:
                for par in range(2):
                    sp.wait_ge(wd_split, 2 * (p - 1) + par + 1)
                    sp.dma_start(w_raw[par][:, :], w_dram[bass.ds(2 * p + par, 1), :, :]
                                 .rearrange("a p c -> p (a c)")).then_inc(w_in[par], 16)
                sp.wait_ge(wt_split, p)
                sp.dma_start(wt_raw[:, :], wtail_dram[bass.ds(p, 1), :, :]
                             .rearrange("a p c -> p (a c)")).then_inc(wt_in, 16)
            for h in range(HALVES):
                sp.wait_ge(out_ready, h + 1)
                sp.dma_start(out_dram[:, :, h * HALF:(h + 1) * HALF], out_sb[:, h, :, :]).then_inc(out_stored, 16)
            sp.wait_ge(out_stored, 16 * HALVES)

        @block.gpsimd
        def _(pool):
            nc.gpsimd.memset(ident[:, :], 0.0).then_inc(pool_step, 1)
            nc.gpsimd.iota(adapter_i[:, :], [[0, 1]], base=0, channel_multiplier=1).then_inc(pool_step, 1)
            for e in range(EXPERTS):
                nc.gpsimd.memset(tie[:, :].rearrange("p (t e) -> p t e", e=EXPERTS)[:, :, e:e + 1],
                                 float(EXPERTS - 1 - e))
            nc.gpsimd.memset(as_f32(zeros[:, :]), 0.0)
            pool.wait_ge(pool_step, 2)
            nc.gpsimd.affine_select(out=ident[:, :], in_=ident[:, :], compare_op=ALU.not_equal, fill=1.0, base=0,
                                    pattern=[[-1, P]], channel_multiplier=1).then_inc(consts_ready, 1)

            def split(raw, hi, lo, count, done):
                nc.gpsimd.tensor_copy(hi, raw).then_inc(whi_step, 1)
                pool.wait_ge(whi_step, count)
                nc.gpsimd.tensor_tensor(lo, raw, as_f32(hi), ALU.subtract).then_inc(done, 1)

            def split_pair(p):
                for par in range(2):
                    pool.wait_ge(w_in[par], 16 * (p + 1))
                    for k, (cols, done) in enumerate(((slice(0, DOWN_AT), wgu_split),
                                                      (slice(DOWN_AT, W_COLS), wd_split))):
                        split(w_raw[par][:, cols], w_hi[par][:, cols], w_lo[par][:, cols],
                              5 * p + 2 * par + k + 1, done)
                    yield par
                pool.wait_ge(wt_in, 16 * (p + 1))
                split(wt_raw[:, :], wt_hi[:, :], wt_lo[:, :], 5 * p + 5, wt_split)

            for p in range(PAIRS):
                if p > 0:
                    pool.wait_ge(downs_done, DOWNS * (p - 1) + downs_through(2 * PER_UNIT - 2))
                for par in split_pair(p):
                    if par == 0 and p > 0:
                        pool.wait_ge(downs_done, DOWNS * p)

        @block.scalar
        def _(act):
            act.dma_start(pack[:, :], pack_dram[:, :]).then_inc(pack_in, 16)
            act.dma_start(idx[:, :], idx_dram[:, :]).then_inc(idx_in, 16)
            act.wait_ge(pack_in, 16)
            nc.scalar.activation(pk_hi[:, :], pack[:, 0:PK_S], ACT.Copy).then_inc(pk_hi_ready, 1)
            for h in range(HALVES):
                tok = slice(h * HALF, (h + 1) * HALF)
                act.wait_ge(x_in[h], 16)
                nc.scalar.activation(x_hi[:, :, tok], x[:, :, tok], ACT.Copy).then_inc(x_hi_ready, 1)
            for h in range(HALVES):
                tok = slice(h * HALF, (h + 1) * HALF)
                act.wait_ge(xa_masked, h + 1)
                nc.scalar.activation(xa_hi[:, tok], xa[:, tok], ACT.Copy).then_inc(xa_hi_ready, 1)
            for h in range(HALVES):
                tok = slice(h * HALF, (h + 1) * HALF)
                act.wait_ge(cond_done, h + 1)
                nc.scalar.activation(c_hi[:, :, tok], acc[:, h, :, :], ACT.Copy).then_inc(c_hi_ready, 1)
            act.wait_ge(combT_done, 1)
            nc.scalar.activation(combT[:, :].rearrange("e (h t) -> e h t", h=HALVES),
                                 acc[0:EXPERTS, 0, :, :], ACT.Copy).then_inc(combT_copied, 1)

            with act.Fori(0, PAIRS) as p:
                for n in range(ITEMS):
                    par, half, j = unit_of(n)
                    rows = slice(0, P) if j < FULL else slice(par * TAIL, par * TAIL + TAIL)
                    src = gate_ps[n % 2][:, :] if j < FULL else gate_ps[n % 2][0:TAIL, :]
                    act.wait_ge(gates_done, ITEMS * p + n + 1)
                    nc.scalar.activation(sg[n % 2][rows, :], src, ACT.Silu).then_inc(silu_done, 1)
                    hi, _, _ = item_buffers(n, h_hi, h_lo)
                    act.wait_ge(hidc_done, ITEMS * p + n + 1)
                    nc.scalar.activation(hi, hidc[rows, :], ACT.Copy).then_inc(h_hi_ready, 1)

        @block.vector
        def _(dve):
            steps = [0]

            def chain(ins):
                steps[0] += 1
                ins.then_inc(dve_step, 1)
                dve.wait_ge(dve_step, steps[0])

            dve.wait_ge(consts_ready, 1)
            chain(nc.vector.tensor_scalar(adapter_i[:, :], adapter_i[:, :], 4, None, ALU.arith_shift_right))
            dve.wait_ge(idx_in, 16)
            chain(nc.vector.tensor_copy(adapter_f[:, :], adapter_i[:, :]))
            chain(nc.vector.tensor_copy(idx_f[:, :], idx[:, :]))
            dve.wait_ge(pack_in, 16)
            chain(nc.vector.tensor_scalar(adapter_mask[:, :], idx_f[:, :], adapter_f[:, :],
                                          pack[:, PK_S:PK_S + 1], ALU.is_equal, ALU.mult))
            dve.wait_ge(pk_hi_ready, 1)
            nc.vector.tensor_tensor(pk_lo[:, :], pack[:, 0:PK_S], as_f32(pk_hi[:, :]),
                                    ALU.subtract).then_inc(pk_lo_ready, 1)
            for h in range(HALVES):
                tok = slice(h * HALF, (h + 1) * HALF)
                dve.wait_ge(x_hi_ready, h + 1)
                nc.vector.tensor_tensor(x_lo[:, :, tok], x[:, :, tok], as_f32(x_hi[:, :, tok]),
                                        ALU.subtract).then_inc(x_lo_ready, 1)
            nb = HALF // SEQ
            for h in range(HALVES):
                tok = slice(h * HALF, (h + 1) * HALF)
                dve.wait_ge(xa_done, h + 1)
                nc.vector.tensor_tensor(
                    xa[:, tok].rearrange("p (b s) -> p b s", s=SEQ),
                    gate_ps[h][:, :].rearrange("p (b s) -> p b s", s=SEQ),
                    adapter_mask[:, h * nb:(h + 1) * nb].unsqueeze(2).broadcast_to([P, nb, SEQ]),
                    ALU.mult).then_inc(xa_masked, 1)
            for h in range(HALVES):
                tok = slice(h * HALF, (h + 1) * HALF)
                dve.wait_ge(xa_hi_ready, h + 1)
                nc.vector.tensor_tensor(xa_lo[:, tok], xa[:, tok], as_f32(xa_hi[:, tok]),
                                        ALU.subtract).then_inc(xa_lo_ready, 1)
            for h in range(HALVES):
                tok = slice(h * HALF, (h + 1) * HALF)
                dve.wait_ge(c_hi_ready, h + 1)
                nc.vector.tensor_tensor(c_lo[:, :, tok], acc[:, h, :, :], as_f32(c_hi[:, :, tok]),
                                        ALU.subtract).then_inc(c_lo_ready, 1)

            def full(i):
                return rt[:, i, :]

            def by_tile(i):
                return rt[:, i, :].rearrange("p (t e) -> p t e", e=EXPERTS)

            def spread(i):
                return rs[:, i, :].unsqueeze(2).broadcast_to([P, TILES, EXPERTS])

            shifted, poly, weights, key, key2, picked = 0, 1, 2, 3, 4, 5
            dve.wait_ge(logits_done, 1)
            ins = nc.vector.tensor_scalar(full(shifted), up_ps[1][:, 0:TILES * EXPERTS], Q_IN, ROUND_SIGNED,
                                          ALU.mult, ALU.add)
            chain(ins)
            nc.vector.sem_inc(logits_read, 1)
            chain(nc.vector.tensor_scalar(full(shifted), full(shifted), ROUND_SIGNED, None, ALU.subtract))
            chain(nc.vector.tensor_reduce(rs[:, 0, :], by_tile(shifted), AX_X, ALU.max))
            chain(nc.vector.tensor_tensor(by_tile(shifted), by_tile(shifted), spread(0), ALU.subtract))
            chain(nc.vector.tensor_scalar(full(shifted), full(shifted), LUT_MIN, -LUT_MIN / 2, ALU.max, ALU.add))
            chain(nc.vector.tensor_scalar(full(poly), full(shifted), EXP_POLY[0], None, ALU.mult))
            for c in EXP_POLY[1:-1]:
                chain(nc.vector.scalar_tensor_tensor(full(poly), full(poly), c, full(shifted), ALU.add, ALU.mult))
            chain(nc.vector.tensor_scalar(full(poly), full(poly), EXP_POLY[-1], -0.5, ALU.add, ALU.add))
            chain(nc.vector.tensor_scalar(full(poly), full(poly), ROUND_POSITIVE, ROUND_POSITIVE,
                                          ALU.add, ALU.subtract))
            chain(nc.vector.tensor_reduce(rs[:, 1, :], by_tile(poly), AX_X, ALU.add))
            chain(nc.vector.tensor_scalar(rs[:, 1, :], rs[:, 1, :], 1.0, None, ALU.max))
            chain(nc.vector.reciprocal(rs[:, 2, :], rs[:, 1, :]))
            chain(nc.vector.tensor_tensor(by_tile(weights), by_tile(poly), spread(2), ALU.mult))
            dve.wait_ge(consts_ready, 1)
            chain(nc.vector.scalar_tensor_tensor(full(key), full(poly), float(EXPERTS), tie[:, :], ALU.mult, ALU.add))
            chain(nc.vector.tensor_reduce(rs[:, 3, :], by_tile(key), AX_X, ALU.max))
            chain(nc.vector.tensor_tensor(by_tile(key2), by_tile(key), spread(3), ALU.is_lt))
            chain(nc.vector.tensor_tensor(full(key2), full(key2), full(key), ALU.mult))
            chain(nc.vector.tensor_reduce(rs[:, 4, :], by_tile(key2), AX_X, ALU.max))
            chain(nc.vector.tensor_tensor(by_tile(picked), by_tile(key), spread(4), ALU.is_ge))
            chain(nc.vector.tensor_tensor(full(weights), full(weights), full(picked), ALU.mult))
            chain(nc.vector.tensor_reduce(rs[:, 5, :], by_tile(weights), AX_X, ALU.add))
            chain(nc.vector.reciprocal(rs[:, 0, :], rs[:, 5, :]))
            nc.vector.tensor_tensor(by_tile(key), by_tile(weights), spread(0), ALU.mult).then_inc(combine_ready, 1)

            dve.wait_ge(comb_first_in, 16)
            with dve.Fori(0, PAIRS) as p:
                for n in range(ITEMS):
                    par, half, j = unit_of(n)
                    hi, lo, rows = item_buffers(n, h_hi, h_lo)
                    up = up_ps[n % 2][:, :] if j < FULL else gate_ps[n % 2][TAIL:2 * TAIL, :]
                    if j < FULL:
                        dve.wait_ge(ups_done, FULLS * p + fulls_through(n))
                    dve.wait_ge(silu_done, ITEMS * p + n + 1)
                    nc.vector.tensor_tensor(hid[rows, :], up, sg[n % 2][rows, :], ALU.mult).then_inc(hid_done, 1)
                    if n == 2 * PER_UNIT:
                        dve.wait_ge(comb_rest_in, 16)
                    dve.wait_ge(hid_done, ITEMS * p + n + 1)
                    at = (2 * p + par) * TOKENS + half * HALF
                    nc.vector.tensor_tensor(hidc[rows, :], hid[rows, :], comb[rows, bass.ds(at, HALF)],
                                            ALU.mult).then_inc(hidc_done, 1)
                    dve.wait_ge(h_hi_ready, ITEMS * p + n + 1)
                    nc.vector.tensor_tensor(lo, hidc[rows, :], as_f32(hi), ALU.subtract).then_inc(h_lo_ready, 1)

            for h in range(HALVES):
                last_item = (2 + h) * PER_UNIT + PER_UNIT - 1
                dve.wait_ge(downs_done, DOWNS * (PAIRS - 1) + downs_through(last_item))
                nc.vector.tensor_tensor(out_sb[:, h, :, :], acc[:, h, :, :], x[:, :, h * HALF:(h + 1) * HALF],
                                        ALU.add).then_inc(out_ready, 1)

        @block.tensor
        def _(pe):
            def product(out, terms, start, stop):
                passes = [q for whi, wlo, vhi, vlo in terms for q in ((wlo, vhi), (whi, vlo), (whi, vhi))]
                for i, (w, v) in enumerate(passes):
                    last = nc.tensor.matmul(out, w, v, start=start and i == 0, stop=stop and i == len(passes) - 1)
                return last

            def small(at, width, kc_step, kc):
                cols = slice(at + kc * kc_step, at + kc * kc_step + width)
                return pk_hi[:, cols], pk_lo[:, cols]

            pe.wait_ge(pk_lo_ready, 1)
            for h in range(HALVES):
                tok = slice(h * HALF, (h + 1) * HALF)
                pe.wait_ge(x_lo_ready, h + 1)
                product(gate_ps[h][:, :],
                        [(*small(PK_A, P, P, kc), x_hi[:, kc, tok], x_lo[:, kc, tok]) for kc in range(KC)],
                        True, True).then_inc(xa_done, 1)
            for h in range(HALVES):
                tok = slice(h * HALF, (h + 1) * HALF)
                for oc in range(KC):
                    product(acc[:, h, oc, :],
                            [(*small(PK_W + oc * P, P, DIM, kc), x_hi[:, kc, tok], x_lo[:, kc, tok])
                             for kc in range(KC)], True, False)
            for h in range(HALVES):
                tok = slice(h * HALF, (h + 1) * HALF)
                pe.wait_ge(xa_lo_ready, h + 1)
                for oc in range(KC):
                    last = product(acc[:, h, oc, :], [(*small(PK_B + oc * P, P, 0, 0), xa_hi[:, tok], xa_lo[:, tok])],
                                   False, True)
                last.then_inc(cond_done, 1)
            for t in range(TILES):
                tok = slice(t * P, (t + 1) * P)
                if t % (TILES // HALVES) == 0:
                    pe.wait_ge(c_lo_ready, t // (TILES // HALVES) + 1)
                last = product(up_ps[1][:, t * EXPERTS:(t + 1) * EXPERTS],
                               [(c_hi[:, kc, tok], c_lo[:, kc, tok], *small(PK_G, EXPERTS, EXPERTS, kc))
                                for kc in range(KC)], True, True)
            last.then_inc(logits_done, 1)

            def gate_up(n, p):
                par, half, j = unit_of(n)
                tok = slice(half * HALF, (half + 1) * HALF)
                if n % (2 * PER_UNIT) == 0:
                    pe.wait_ge(wgu_split, 2 * p + par + 1)

                def cols(at):
                    return [(w_hi[par][:, kc * GU_COLS + at:kc * GU_COLS + at + P],
                             w_lo[par][:, kc * GU_COLS + at:kc * GU_COLS + at + P],
                             c_hi[:, kc, tok], c_lo[:, kc, tok]) for kc in range(KC)]

                if j < FULL:
                    product(gate_ps[n % 2][:, :], cols(j * P), True, True).then_inc(gates_done, 1)
                    product(up_ps[n % 2][:, :], cols(UP_AT + j * P), True, True).then_inc(ups_done, 1)
                else:
                    product(gate_ps[n % 2][:, :], cols(TAILS_AT), True, True).then_inc(gates_done, 1)

            def down(n, p, last_pair):
                par, half, j = unit_of(n)
                if not has_down(n):
                    return
                pe.wait_ge(h_lo_ready, ITEMS * p + n + 1)
                if j < FULL:
                    if n % (2 * PER_UNIT) == 0:
                        pe.wait_ge(wd_split, 2 * p + par + 1)
                    at, whi, wlo, hhi, hlo = DOWN_AT + j * DIM, w_hi[par], w_lo[par], h_hi[n % RING], h_lo[n % RING]
                else:
                    if half == 0:
                        pe.wait_ge(wt_split, p + 1)
                    at, whi, wlo, hhi, hlo = 0, wt_hi, wt_lo, t_hi[half], t_lo[half]
                for oc in range(KC):
                    cols = slice(at + oc * P, at + oc * P + P)
                    last = product(acc[:, half, oc, :], [(whi[:, cols], wlo[:, cols], hhi[:, :], hlo[:, :])],
                                   False, last_pair and par == 1 and j == FULL)
                last.then_inc(downs_done, 1)

            gate_up(0, 0)
            pe.wait_ge(logits_read, 1)
            gate_up(1, 0)
            pe.wait_ge(combine_ready, 1)
            pe.wait_ge(consts_ready, 1)
            for t in range(TILES):
                bank, at = divmod(t * P, HALF)
                last = nc.tensor.matmul(acc[0:EXPERTS, 0, bank, at:at + P], rt[:, 3, t * EXPERTS:(t + 1) * EXPERTS],
                                        ident[:, :], start=True, stop=True)
            last.then_inc(combT_done, 1)
            pe.wait_ge(combT_copied, 1)
            for h in range(HALVES):
                for oc in range(KC):
                    nc.tensor.matmul(acc[:, h, oc, :], zeros[:, 0:P], zeros[:, :], start=True, stop=False)

            def pair(p, last_pair):
                for n in range(ITEMS):
                    ahead = n + LAG
                    if ahead < ITEMS or not last_pair:
                        q = p if ahead < ITEMS else p + 1
                        pe.wait_ge(hid_done, ITEMS * p + ahead - 1)
                        gate_up(ahead % ITEMS, q)
                    down(n, p, last_pair)

            with pe.Fori(0, PAIRS - 1) as p:
                pair(p, False)
            pair(PAIRS - 1, True)


def kernel(**inputs):
    import numpy as np
    import concourse.bacc as bacc
    from concourse.bass_utils import run_bass_kernel_spmd

    def chunked(a):
        return a.reshape(KC, P, *a.shape[1:]).swapaxes(0, 1)

    x = np.asarray(inputs["x"]).reshape(TOKENS, DIM)
    scal = np.repeat(np.asarray(inputs["L0_cond_scalings"]), RANK).reshape(P, 1)
    pack = np.concatenate([
        chunked(np.asarray(inputs["L0_cond_W"]).T).reshape(P, KC * DIM),
        chunked(np.asarray(inputs["L0_cond_A"]).reshape(ADAPTERS * RANK, DIM).T).reshape(P, KC * P),
        np.asarray(inputs["L0_cond_Bm"]).transpose(0, 2, 1).reshape(ADAPTERS * RANK, DIM),
        chunked(np.asarray(inputs["L0_ffn_w_gate"]).T).reshape(P, KC * EXPERTS),
        scal], axis=1)
    w1, w2, w3 = (np.asarray(inputs[f"L0_ffn_w{i}"]) for i in (1, 2, 3))
    body = FULL * P
    gate, up = w1.transpose(0, 2, 1), w3.transpose(0, 2, 1)
    gu = np.concatenate([gate[:, :, :body], up[:, :, :body], gate[:, :, body:], up[:, :, body:]], axis=2)
    gu = gu.reshape(EXPERTS, KC, P, GU_COLS).transpose(0, 2, 1, 3).reshape(EXPERTS, P, KC * GU_COLS)
    dn = w2.transpose(0, 2, 1)
    dn_full = dn[:, :body].reshape(EXPERTS, FULL, P, DIM).transpose(0, 2, 1, 3).reshape(EXPERTS, P, FULL * DIM)
    arrays = {
        "x_t": chunked(x.T),
        "small_weights": pack,
        "adapter_of_batch": np.broadcast_to(np.asarray(inputs["itok_B_0_6"]), (P, BATCH)),
        "expert_weights": np.concatenate([gu, dn_full], axis=2),
        "tail_down_weights": dn[:, body:].reshape(PAIRS, P, DIM),
    }
    arrays = {k: np.ascontiguousarray(v) for k, v in arrays.items()}

    nc = bacc.Bacc("TRN2", target_bir_lowering=False, num_devices=1)
    args = [nc.dram_tensor(k, v.shape, mybir.dt.from_np(v.dtype), kind="ExternalInput").ap()
            for k, v in arrays.items()]
    comb_dram = nc.dram_tensor("combine_t", (EXPERTS, TOKENS), F32, kind="Internal").ap()
    out = nc.dram_tensor("out_t", (P, KC, TOKENS), F32, kind="ExternalOutput").ap()
    moe_kernel(nc, *args, comb_dram, out)
    got = run_bass_kernel_spmd(nc, [arrays], core_ids=[0]).results[0]["out_t"]
    return got.transpose(1, 0, 2).reshape(DIM, TOKENS).T.reshape(BATCH, SEQ, DIM)
```

```python
from contextlib import ExitStack

import concourse.bass as bass
from concourse import mybir

P = 128
TOKENS = 1024
DIM = 256
KC = DIM // P
HALF = 512
HALVES = TOKENS // HALF
BATCH, SEQ = 32, 32
ADAPTERS, RANK = 8, 16
EXPERTS = 8
HIDDEN = 704
FULL = HIDDEN // P
TAIL = HIDDEN - FULL * P
TILES = TOKENS // P
PAIRS = EXPERTS // 2

ITEM_COLS = 2 * KC * P
TAILS_AT = FULL * ITEM_COLS
DOWN_AT = TAILS_AT + KC * 2 * TAIL
W_COLS = DOWN_AT + FULL * DIM
FIRST_ITEMS = 2
PIECES = [slice(0, FIRST_ITEMS * ITEM_COLS), slice(FIRST_ITEMS * ITEM_COLS, DOWN_AT), slice(DOWN_AT, W_COLS)]

PK_A = 0
PK_W = PK_A + KC * P
PK_B = PK_W + KC * DIM
PK_G = PK_B + DIM
PK_S = PK_G + KC * EXPERTS
PK_COLS = PK_S + 1

UNITS = 4
PER_UNIT = FULL + 1
ITEMS = UNITS * PER_UNIT
FULLS = UNITS * FULL
DOWNS = ITEMS - 2
LAST_ITEM = [(2 + h) * PER_UNIT + PER_UNIT - 1 for h in range(2)]
LAG = 4
AHEAD = 2
RING = 6
HIDS = 4
WARM_UP = 11

Q_IN = 128.0
LUT_MIN = -128.0
EXP_POLY = [1.2659316303564871e-11, 9.735014572243017e-09, 6.169693278934574e-06,
            0.0031588352285325527, 1.2130615711212158, 310.5437927246094, 39749.59375]
KEY_OFFSET = 8.0 * (1 - LUT_MIN / 2)
ROUND_SIGNED = 1.5 * 2.0 ** 23
ROUND_POSITIVE = 2.0 ** 23

ALU = mybir.AluOpType
ACT = mybir.ActivationFunctionType
F32 = mybir.dt.float32
F32R = mybir.dt.float32r
I32 = mybir.dt.int32
AX_X = mybir.AxisListType.X


def unit_of(n):
    return n // (2 * PER_UNIT), (n // PER_UNIT) % 2, n % PER_UNIT


def has_down(n):
    par, _, j = unit_of(n)
    return par == 1 or j < FULL


def next_ahead(n, last_pair):
    if not last_pair or n + AHEAD < ITEMS - 1:
        return n + AHEAD
    return ITEMS - 1 if n == ITEMS - 2 else None


def fulls_through(n):
    return sum(unit_of(m)[2] < FULL for m in range(n + 1))


def downs_through(n):
    return sum(has_down(m) for m in range(n + 1))


def moe_kernel(nc, x_dram, pack_dram, idx_dram, w_dram, wtail_dram, comb_dram, out_dram):
    with ExitStack() as ctx:
        def sb(name, shape, dt=F32):
            return ctx.enter_context(nc.sbuf_tensor(name, shape, dt))

        def ps(name, shape):
            return ctx.enter_context(nc.psum_tensor(name, shape, F32))

        def sem(name):
            return ctx.enter_context(nc.semaphore(name))

        x = sb("x", [P, KC, TOKENS])
        idx = sb("idx", [P, BATCH], I32)
        idx_f = sb("idx_f", [P, BATCH])
        adapter_i = sb("adapter_i", [P, 1], I32)
        adapter_f = sb("adapter_f", [P, 1])
        adapter_mask = sb("adapter_mask", [P, BATCH])
        c_hi = sb("c_hi", [P, KC, TOKENS], F32R)
        c_lo = sb("c_lo", [P, KC, TOKENS], F32R)
        ident = sb("ident", [P, P])
        zeros = sb("zeros", [P, P], F32R)
        tie = sb("tie", [P, TILES * EXPERTS])
        rt = sb("rt", [P, 7, TILES * EXPERTS])
        rs = sb("rs", [P, 6, TILES])
        comb_et = sb("comb_et", [P, EXPERTS, TILES])
        combT = sb("combT", [EXPERTS * TILES, P])
        w_raw = [sb(f"w_raw{i}", [P, W_COLS]) for i in range(2)]
        w_hi = [sb(f"w_hi{i}", [P, W_COLS], F32R) for i in range(2)]
        w_lo = [sb(f"w_lo{i}", [P, W_COLS], F32R) for i in range(2)]
        wt_raw = sb("wt_raw", [P, DIM])
        wt_hi = sb("wt_hi", [P, DIM], F32R)
        wt_lo = sb("wt_lo", [P, DIM], F32R)
        sg = [sb(f"sg{i}", [P, HALF]) for i in range(2)]
        hid = [sb(f"hid{i}", [P, HALF]) for i in range(HIDS)]
        hidc = [sb(f"hidc{i}", [P, HALF]) for i in range(2)]
        h_hi = [sb(f"h_hi{i}", [P, HALF], F32R) for i in range(RING)]
        h_lo = [sb(f"h_lo{i}", [P, HALF], F32R) for i in range(RING)]
        t_hi = [sb(f"t_hi{i}", [P, HALF], F32R) for i in range(HALVES)]
        t_lo = [sb(f"t_lo{i}", [P, HALF], F32R) for i in range(HALVES)]
        with ExitStack() as early:
            def sb_early(name, shape, dt=F32):
                return early.enter_context(nc.sbuf_tensor(name, shape, dt))

            x_hi = sb_early("x_hi", [P, KC, TOKENS], F32R)
            x_lo = sb_early("x_lo", [P, KC, TOKENS], F32R)
            pack = sb_early("pack", [P, PK_COLS])
            pk_hi = sb_early("pk_hi", [P, PK_G], F32R)
            pk_lo = sb_early("pk_lo", [P, PK_G], F32R)
            g_both = sb_early("g_both", [P, KC, 2, EXPERTS], F32R)
        router_w = pack[:, PK_G:PK_S].rearrange("p (c e) -> p c e", e=EXPERTS)
        comb = sb("comb", [P, EXPERTS * TOKENS])
        xa, xa_hi, xa_lo = hid[0:HALVES], h_hi[0:HALVES], h_lo[0:HALVES]
        out_sb = [[comb[:, (KC * h + oc) * HALF:(KC * h + oc + 1) * HALF] for oc in range(KC)]
                  for h in range(HALVES)]

        acc = ps("acc", [P, HALVES, KC, HALF])
        gate_ps = [ps(f"gate_ps{i}", [P, HALF]) for i in range(2)]
        up_ps = [ps(f"up_ps{i}", [P, HALF]) for i in range(2)]

        x_in = [sem(f"x_in{i}") for i in range(3)]
        pack_a_in = sem("pack_a_in")
        pack_in = sem("pack_in")
        idx_in = sem("idx_in")
        w_first_in = sem("w_first_in")
        w_in = [sem(f"w_in{i}") for i in range(2)]
        wt_in = sem("wt_in")
        consts_ready = sem("consts_ready")
        zeros_ready = sem("zeros_ready")
        pool_step = sem("pool_step")
        pk_hi_ready = sem("pk_hi_ready")
        pk_lo_ready = sem("pk_lo_ready")
        g_hi_ready = sem("g_hi_ready")
        g_lo_ready = sem("g_lo_ready")
        x_hi_ready = sem("x_hi_ready")
        x_lo_ready = sem("x_lo_ready")
        xa_done = sem("xa_done")
        xa_masked = sem("xa_masked")
        xa_hi_ready = sem("xa_hi_ready")
        xa_lo_ready = sem("xa_lo_ready")
        cond_done = sem("cond_done")
        c_hi_ready = sem("c_hi_ready")
        c_lo_ready = sem("c_lo_ready")
        logits_done = sem("logits_done")
        logits_read = sem("logits_read")
        dve_step = sem("dve_step")
        combine_ready = sem("combine_ready")
        spread_done = sem("spread_done")
        spread_copied = sem("spread_copied")
        combT_done = sem("combT_done")
        combT_copied = sem("combT_copied")
        combT_stored = sem("combT_stored")
        comb_first_in = sem("comb_first_in")
        comb_rest_in = sem("comb_rest_in")
        w_hi_first = sem("w_hi_first")
        w_split = sem("w_split")
        wt_split = sem("wt_split")
        whi_step = sem("whi_step")
        gates_done = sem("gates_done")
        ups_done = sem("ups_done")
        silu_done = sem("silu_done")
        hid_done = sem("hid_done")
        hidc_done = sem("hidc_done")
        h_hi_ready = sem("h_hi_ready")
        h_lo_ready = sem("h_lo_ready")
        downs_done = sem("downs_done")
        last_oc_done = sem("last_oc_done")
        out_ready = sem("out_ready")
        out_stored = sem("out_stored")

        def tok_of(h):
            return slice(h * HALF, (h + 1) * HALF)

        def as_f32(ap):
            return ap.bitcast(F32)

        def item_buffers(n, hi, lo):
            par, half, j = unit_of(n)
            if j < FULL:
                return hi[n % RING][:, :], lo[n % RING][:, :], slice(0, P)
            rows = slice(par * TAIL, par * TAIL + TAIL)
            return t_hi[half][rows, :], t_lo[half][rows, :], rows

        block = ctx.enter_context(nc.Block())

        @block.sync
        def _(sp):
            for kc in range(KC):
                sp.dma_start(x[:, kc, 0:HALF], x_dram[:, kc, 0:HALF]).then_inc(x_in[kc], 16)
            sp.dma_start(x[:, :, HALF:], x_dram[:, :, HALF:]).then_inc(x_in[2], 16)
            first, others = PIECES[0], slice(PIECES[0].stop, W_COLS)
            sp.dma_start(w_raw[0][:, first], w_dram[0, :, first]).then_inc(w_first_in, 16)
            sp.dma_start(w_raw[0][:, others], w_dram[0, :, others]).then_inc(w_in[0], 16)
            sp.dma_start(w_raw[1][:, :], w_dram[1, :, :]).then_inc(w_in[1], 16)
            sp.dma_start(wt_raw[:, :], wtail_dram[0, :, :]).then_inc(wt_in, 16)
            sp.wait_ge(combT_copied, 1)
            sp.dma_start(comb_dram.rearrange("e (t k) -> (e t) k", k=P), combT[:, :]).then_inc(combT_stored, 16)
            sp.wait_ge(combT_stored, 16)
            flat = comb_dram.rearrange("(a e) t -> a (e t)", a=1)
            sp.dma_start(comb[:, HALF:TOKENS],
                         flat[:, HALF:TOKENS].broadcast_to([P, TOKENS - HALF])).then_inc(comb_first_in, 16)
            sp.dma_start(comb[:, TOKENS:],
                         flat[:, TOKENS:].broadcast_to([P, (EXPERTS - 1) * TOKENS])).then_inc(comb_rest_in, 16)
            with sp.Fori(1, PAIRS) as p:
                for par in range(2):
                    sp.wait_ge(w_split, len(PIECES) * (2 * (p - 1) + par + 1))
                    sp.dma_start(w_raw[par][:, :], w_dram[bass.ds(2 * p + par, 1), :, :]
                                 .rearrange("a p c -> p (a c)")).then_inc(w_in[par], 16)
                sp.wait_ge(wt_split, p)
                sp.dma_start(wt_raw[:, :], wtail_dram[bass.ds(p, 1), :, :]
                             .rearrange("a p c -> p (a c)")).then_inc(wt_in, 16)
            for h in range(HALVES):
                for oc in range(KC):
                    sp.wait_ge(out_ready, KC * h + oc + 1)
                    sp.dma_start(out_dram[:, oc, h * HALF:(h + 1) * HALF],
                                 out_sb[h][oc]).then_inc(out_stored, 16)
            sp.wait_ge(out_stored, 16 * HALVES * KC)

        @block.gpsimd
        def _(pool):
            nc.gpsimd.memset(as_f32(zeros[:, :]), 0.0).then_inc(zeros_ready, 1)
            nc.gpsimd.memset(ident[:, :], 0.0).then_inc(pool_step, 1)
            nc.gpsimd.iota(adapter_i[:, :], [[0, 1]], base=0, channel_multiplier=1).then_inc(pool_step, 1)
            for e in range(EXPERTS):
                nc.gpsimd.memset(tie[:, :].rearrange("p (t e) -> p t e", e=EXPERTS)[:, :, e:e + 1],
                                 KEY_OFFSET + EXPERTS - 1 - e)
            pool.wait_ge(pool_step, 2)
            nc.gpsimd.affine_select(out=ident[:, :], in_=ident[:, :], compare_op=ALU.not_equal, fill=1.0, base=0,
                                    pattern=[[-1, P]], channel_multiplier=1).then_inc(consts_ready, 1)

            def lo_part(raw, hi, lo, done):
                nc.gpsimd.tensor_tensor(lo, raw, as_f32(hi), ALU.subtract).then_inc(done, 1)

            steps = 0
            for e in range(EXPERTS):
                par, p = e % 2, e // 2
                if e > 0:
                    pool.wait_ge(w_in[par], 16 * (p + 1))
                if p > 0:
                    pool.wait_ge(downs_done, DOWNS * (p - 1) + downs_through(2 * (par + 1) * PER_UNIT - 1))
                for k, cols in enumerate(PIECES):
                    raw, hi, lo = w_raw[par][:, cols], w_hi[par][:, cols], w_lo[par][:, cols]
                    if e == 0:
                        pool.wait_ge(w_hi_first, k + 1)
                    else:
                        steps += 1
                        nc.gpsimd.tensor_copy(hi, raw).then_inc(whi_step, 1)
                        pool.wait_ge(whi_step, steps)
                    lo_part(raw, hi, lo, w_split)
                if par == 1:
                    steps += 1
                    pool.wait_ge(wt_in, 16 * (p + 1))
                    nc.gpsimd.tensor_copy(wt_hi[:, :], wt_raw[:, :]).then_inc(whi_step, 1)
                    pool.wait_ge(whi_step, steps)
                    lo_part(wt_raw[:, :], wt_hi[:, :], wt_lo[:, :], wt_split)

        @block.scalar
        def _(act):
            act.dma_start(pack[:, 0:PK_W], pack_dram[:, 0:PK_W]).then_inc(pack_a_in, 16)
            act.dma_start(pack[:, PK_W:], pack_dram[:, PK_W:]).then_inc(pack_in, 16)
            act.dma_start(idx[:, :], idx_dram[:, :]).then_inc(idx_in, 16)
            nc.scalar.preload_act_table(ACT.Silu)

            def copy(out, in_):
                return nc.scalar.activation(out, in_, ACT.Copy)

            def xa_hi_part(h):
                act.wait_ge(xa_masked, h + 1)
                copy(xa_hi[h][:, :], xa[h][:, :]).then_inc(xa_hi_ready, 1)

            def c_hi_part(h):
                for oc in range(KC):
                    act.wait_ge(cond_done, KC * h + oc + 1)
                    copy(c_hi[:, oc, tok_of(h)], acc[:, h, oc, :]).then_inc(c_hi_ready, 1)

            def w_hi_part(k):
                act.wait_ge(w_first_in if k == 0 else w_in[0], 16)
                copy(w_hi[0][:, PIECES[k]], w_raw[0][:, PIECES[k]]).then_inc(w_hi_first, 1)

            act.wait_ge(pack_a_in, 16)
            copy(pk_hi[:, 0:PK_W], pack[:, 0:PK_W]).then_inc(pk_hi_ready, 1)
            for kc in range(KC):
                act.wait_ge(x_in[kc], 16)
                copy(x_hi[:, kc, 0:HALF], x[:, kc, 0:HALF]).then_inc(x_hi_ready, 1)
            act.wait_ge(pack_in, 16)
            copy(pk_hi[:, PK_W:], pack[:, PK_W:PK_G]).then_inc(pk_hi_ready, 1)
            copy(g_both[:, :, 0, :], router_w).then_inc(g_hi_ready, 1)
            act.wait_ge(x_in[2], 16)
            copy(x_hi[:, :, HALF:], x[:, :, HALF:]).then_inc(x_hi_ready, 1)
            xa_hi_part(0)
            w_hi_part(0)
            c_hi_part(0)
            xa_hi_part(1)
            w_hi_part(1)
            c_hi_part(1)
            w_hi_part(2)

            def silu(n, p):
                _, _, j = unit_of(n)
                _, _, rows = item_buffers(n, h_hi, h_lo)
                src = gate_ps[n % 2][:, :] if j < FULL else gate_ps[n % 2][0:TAIL, :]
                act.wait_ge(gates_done, ITEMS * p + n + 1)
                nc.scalar.activation(sg[n % 2][rows, :], src, ACT.Silu).then_inc(silu_done, 1)

            for n in range(AHEAD):
                silu(n, 0)
            act.wait_ge(spread_done, 1)
            copy(comb[:, 0:HALF], acc[:, 1, 0, :]).then_inc(spread_copied, 1)
            act.wait_ge(combT_done, 1)
            copy(combT[:, :], acc[0:EXPERTS * TILES, 1, 1, 0:P]).then_inc(combT_copied, 1)

            def pair(p, last_pair):
                for n in range(ITEMS):
                    hi, _, rows = item_buffers(n, h_hi, h_lo)
                    act.wait_ge(hidc_done, ITEMS * p + n + 1)
                    copy(hi, hidc[n % 2][rows, :]).then_inc(h_hi_ready, 1)
                    ahead = next_ahead(n, last_pair)
                    if ahead is not None:
                        silu(ahead % ITEMS, p + ahead // ITEMS)

            with act.Fori(0, PAIRS - 1) as p:
                pair(p, False)
            pair(PAIRS - 1, True)

        @block.vector
        def _(dve):
            steps = [0]

            def chain(ins):
                steps[0] += 1
                ins.then_inc(dve_step, 1)
                dve.wait_ge(dve_step, steps[0])

            def pk_lo_part(cols, count):
                dve.wait_ge(pk_hi_ready, count)
                nc.vector.tensor_tensor(pk_lo[:, cols], pack[:, cols], as_f32(pk_hi[:, cols]),
                                        ALU.subtract).then_inc(pk_lo_ready, 1)

            def x_lo_part(kc, tok, count):
                dve.wait_ge(x_hi_ready, count)
                nc.vector.tensor_tensor(x_lo[:, kc, tok], x[:, kc, tok], as_f32(x_hi[:, kc, tok]),
                                        ALU.subtract).then_inc(x_lo_ready, 1)

            nb = HALF // SEQ

            def mask_part(h):
                dve.wait_ge(xa_done, h + 1)
                nc.vector.tensor_tensor(
                    xa[h][:, :].rearrange("p (b s) -> p b s", s=SEQ),
                    gate_ps[h][:, :].rearrange("p (b s) -> p b s", s=SEQ),
                    adapter_mask[:, h * nb:(h + 1) * nb].unsqueeze(2).broadcast_to([P, nb, SEQ]),
                    ALU.mult).then_inc(xa_masked, 1)
                dve.wait_ge(xa_hi_ready, h + 1)
                nc.vector.tensor_tensor(xa_lo[h][:, :], xa[h][:, :], as_f32(xa_hi[h][:, :]),
                                        ALU.subtract).then_inc(xa_lo_ready, 1)

            def c_lo_part(h):
                for oc in range(KC):
                    dve.wait_ge(c_hi_ready, KC * h + oc + 1)
                    nc.vector.tensor_tensor(c_lo[:, oc, tok_of(h)], acc[:, h, oc, :],
                                            as_f32(c_hi[:, oc, tok_of(h)]), ALU.subtract).then_inc(c_lo_ready, 1)

            pk_lo_part(slice(0, PK_W), 1)
            for kc in range(KC):
                x_lo_part(kc, slice(0, HALF), kc + 1)
            pk_lo_part(slice(PK_W, PK_G), 2)
            dve.wait_ge(g_hi_ready, 1)
            nc.vector.tensor_tensor(g_both[:, :, 1, :], router_w, as_f32(g_both[:, :, 0, :]),
                                    ALU.subtract).then_inc(g_lo_ready, 1)
            dve.wait_ge(consts_ready, 1)
            chain(nc.vector.tensor_scalar(adapter_i[:, :], adapter_i[:, :], 4, None, ALU.arith_shift_right))
            nc.vector.tensor_copy(adapter_f[:, :], adapter_i[:, :]).then_inc(dve_step, 1)
            steps[0] += 1
            dve.wait_ge(idx_in, 16)
            chain(nc.vector.tensor_copy(idx_f[:, :], idx[:, :]))
            dve.wait_ge(pack_in, 16)
            chain(nc.vector.tensor_scalar(adapter_mask[:, :], idx_f[:, :], adapter_f[:, :],
                                          pack[:, PK_S:PK_S + 1], ALU.is_equal, ALU.mult))
            mask_part(0)
            x_lo_part(slice(0, KC), slice(HALF, TOKENS), KC + 1)
            c_lo_part(0)
            mask_part(1)
            c_lo_part(1)

            def hidden(n, p):
                _, _, j = unit_of(n)
                _, _, rows = item_buffers(n, h_hi, h_lo)
                up = up_ps[n % 2][:, :] if j < FULL else gate_ps[n % 2][TAIL:2 * TAIL, :]
                if j < FULL:
                    dve.wait_ge(ups_done, FULLS * p + fulls_through(n))
                dve.wait_ge(silu_done, ITEMS * p + n + 1)
                nc.vector.tensor_tensor(hid[n % HIDS][rows, :], up, sg[n % 2][rows, :],
                                        ALU.mult).then_inc(hid_done, 1)

            def full(i):
                return rt[:, i, :]

            def by_tile(i):
                return rt[:, i, :].rearrange("p (t e) -> p t e", e=EXPERTS)

            def spread(i):
                return rs[:, i, :].unsqueeze(2).broadcast_to([P, TILES, EXPERTS])

            def beside(ins):
                steps[0] += 1
                ins.then_inc(dve_step, 1)

            z, poly, key, key2, picked, top = range(6)
            most, total, inv_total, key_1, key_2, top_total = range(6)
            logit_parts = up_ps[1][:, 0:2 * TILES * EXPERTS].rearrange("p (t s e) -> p t e s", s=2, e=EXPERTS)
            dve.wait_ge(logits_done, 1)
            nc.vector.tensor_reduce(by_tile(z), logit_parts, AX_X, ALU.add).then_inc(logits_read, 1)
            dve.wait_ge(logits_read, 1)
            chain(nc.vector.tensor_scalar(full(z), full(z), Q_IN, ROUND_SIGNED, ALU.mult, ALU.add))
            chain(nc.vector.tensor_reduce(rs[:, most, :], by_tile(z), AX_X, ALU.max))
            chain(nc.vector.tensor_tensor(by_tile(z), by_tile(z), spread(most), ALU.subtract))
            chain(nc.vector.tensor_scalar(full(z), full(z), LUT_MIN, -LUT_MIN / 2, ALU.max, ALU.add))
            hidden(0, 0)
            beside(nc.vector.tensor_scalar(full(poly), full(z), EXP_POLY[0], None, ALU.mult))
            chain(nc.vector.scalar_tensor_tensor(full(key), full(z), float(EXPERTS), tie[:, :], ALU.mult, ALU.add))
            selection = [
                lambda: nc.vector.tensor_reduce(rs[:, key_1, :], by_tile(key), AX_X, ALU.max),
                lambda: nc.vector.tensor_tensor(by_tile(key2), by_tile(key), spread(key_1), ALU.is_lt),
                lambda: nc.vector.tensor_tensor(full(key2), full(key2), full(key), ALU.mult),
                lambda: nc.vector.tensor_reduce(rs[:, key_2, :], by_tile(key2), AX_X, ALU.max),
                lambda: nc.vector.tensor_tensor(by_tile(picked), by_tile(key), spread(key_2), ALU.is_ge),
            ]
            for c, select in zip(EXP_POLY[1:-1], selection, strict=True):
                beside(nc.vector.scalar_tensor_tensor(full(poly), full(poly), c, full(z), ALU.add, ALU.mult))
                chain(select())
            chain(nc.vector.tensor_scalar(full(poly), full(poly), EXP_POLY[-1], -0.5, ALU.add, ALU.add))
            chain(nc.vector.tensor_scalar(full(poly), full(poly), ROUND_POSITIVE, ROUND_POSITIVE,
                                          ALU.add, ALU.subtract))
            beside(nc.vector.tensor_reduce(rs[:, total, :], by_tile(poly), AX_X, ALU.add))
            chain(nc.vector.tensor_tensor(full(top), full(poly), full(picked), ALU.mult))
            chain(nc.vector.tensor_scalar(rs[:, total, :], rs[:, total, :], 1.0, None, ALU.max))
            chain(nc.vector.reciprocal(rs[:, inv_total, :], rs[:, total, :]))
            chain(nc.vector.tensor_tensor(by_tile(top), by_tile(top), spread(inv_total), ALU.mult))
            chain(nc.vector.tensor_reduce(rs[:, top_total, :], by_tile(top), AX_X, ALU.add))
            chain(nc.vector.reciprocal(rs[:, most, :], rs[:, top_total, :]))
            nc.vector.tensor_tensor(comb_et[:, :, :].rearrange("p e t -> p t e"), by_tile(top), spread(most),
                                    ALU.mult).then_inc(combine_ready, 1)
            hidden(1, 0)

            def residual(h, oc):
                if oc == 0:
                    dve.wait_ge(last_oc_done, h + 1)
                else:
                    dve.wait_ge(downs_done, DOWNS * (PAIRS - 1) + downs_through(LAST_ITEM[h]))
                nc.vector.tensor_tensor(out_sb[h][oc], acc[:, h, oc, :], x[:, oc, tok_of(h)],
                                        ALU.add).then_inc(out_ready, 1)

            def combined(n, p, last_pair):
                par, half, j = unit_of(n)
                _, lo, rows = item_buffers(n, h_hi, h_lo)
                if n == 0:
                    dve.wait_ge(spread_copied, 1)
                if n == PER_UNIT:
                    dve.wait_ge(comb_first_in, 16)
                if n == 2 * PER_UNIT:
                    dve.wait_ge(comb_rest_in, 16)
                dve.wait_ge(hid_done, ITEMS * p + n + 1)
                if n >= 2:
                    dve.wait_ge(h_lo_ready, ITEMS * p + n - 1)
                at = (2 * p + par) * TOKENS + half * HALF
                nc.vector.tensor_tensor(hidc[n % 2][rows, :], hid[n % HIDS][rows, :], comb[rows, bass.ds(at, HALF)],
                                        ALU.mult).then_inc(hidc_done, 1)
                ahead = next_ahead(n, last_pair)
                if ahead == n + AHEAD:
                    hidden(ahead % ITEMS, p + ahead // ITEMS)
                if last_pair and n >= ITEMS - KC:
                    residual(0, n - (ITEMS - KC))
                dve.wait_ge(h_hi_ready, ITEMS * p + n + 1)
                nc.vector.tensor_tensor(lo, hidc[n % 2][rows, :], as_f32(hi_of(n)), ALU.subtract).then_inc(h_lo_ready, 1)
                if ahead == n + 1:
                    hidden(ahead, p)

            def hi_of(n):
                return item_buffers(n, h_hi, h_lo)[0]

            with dve.Fori(0, PAIRS - 1) as p:
                for n in range(ITEMS):
                    combined(n, p, False)
                dve.wait_ge(h_lo_ready, ITEMS * p + ITEMS)
            for n in range(ITEMS):
                combined(n, PAIRS - 1, True)
            for oc in range(KC):
                residual(1, oc)

        @block.tensor
        def _(pe):
            def product(out, terms, start, stop):
                passes = [q for whi, wlo, vhi, vlo in terms for q in ((wlo, vhi), (whi, vlo), (whi, vhi))]
                for i, (w, v) in enumerate(passes):
                    last = nc.tensor.matmul(out, w, v, start=start and i == 0, stop=stop and i == len(passes) - 1)
                return last

            def small(at, width, kc_step, kc):
                cols = slice(at + kc * kc_step, at + kc * kc_step + width)
                return pk_hi[:, cols], pk_lo[:, cols]

            wide_zeros = zeros[:, :].unsqueeze(1).broadcast_to([P, HALF // P, P])

            pe.wait_ge(zeros_ready, 1)
            for _ in range(WARM_UP):
                nc.tensor.matmul(up_ps[0][:, :], zeros[:, :], wide_zeros, start=True, stop=True)

            def adapters(h):
                tok = tok_of(h)
                for kc in range(KC):
                    w_h, w_l = small(PK_A, P, P, kc)
                    pe.wait_ge(x_hi_ready, kc + 1 if h == 0 else KC + 1)
                    if h == kc == 0:
                        pe.wait_ge(pk_hi_ready, 1)
                    nc.tensor.matmul(gate_ps[h][:, :], w_h, x_hi[:, kc, tok], start=kc == 0, stop=False)
                    if h == kc == 0:
                        pe.wait_ge(pk_lo_ready, 1)
                    nc.tensor.matmul(gate_ps[h][:, :], w_l, x_hi[:, kc, tok], start=False, stop=False)
                for kc in range(KC):
                    pe.wait_ge(x_lo_ready, kc + 1 if h == 0 else KC + 1)
                    last = nc.tensor.matmul(gate_ps[h][:, :], small(PK_A, P, P, kc)[0], x_lo[:, kc, tok],
                                            start=False, stop=kc == KC - 1)
                last.then_inc(xa_done, 1)

            def base(h):
                pe.wait_ge(pk_lo_ready, 2)
                for oc in range(KC):
                    product(acc[:, h, oc, :],
                            [(*small(PK_W + oc * P, P, DIM, kc), x_hi[:, kc, tok_of(h)], x_lo[:, kc, tok_of(h)])
                             for kc in range(KC)], True, False)

            def low_rank(h):
                pe.wait_ge(xa_lo_ready, h + 1)
                for oc in range(KC):
                    product(acc[:, h, oc, :],
                            [(*small(PK_B + oc * P, P, 0, 0), xa_hi[h][:, :], xa_lo[h][:, :])],
                            False, True).then_inc(cond_done, 1)

            def logits(h):
                pe.wait_ge(g_lo_ready, 1)
                pe.wait_ge(c_lo_ready, KC * (h + 1))
                for t in range(h * TILES // HALVES, (h + 1) * TILES // HALVES):
                    tok = slice(t * P, (t + 1) * P)
                    at = 2 * EXPERTS * t
                    both = up_ps[1][:, at:at + 2 * EXPERTS]
                    for kc in range(KC):
                        nc.tensor.matmul(both, c_hi[:, kc, tok], g_both[:, kc, :, :].rearrange("p s e -> p (s e)"),
                                         start=kc == 0, stop=False, skip_group_check=True)
                    for kc in range(KC):
                        last = nc.tensor.matmul(both[:, 0:EXPERTS], c_lo[:, kc, tok], g_both[:, kc, 0, :],
                                                start=False, stop=kc == KC - 1, skip_group_check=True)
                if h == HALVES - 1:
                    last.then_inc(logits_done, 1)

            def gate_up(n, p, before_up=None):
                par, half, j = unit_of(n)
                if j == 0 and half == 0:
                    pe.wait_ge(w_split, len(PIECES) * (2 * p + par) + 1)
                if j == FIRST_ITEMS and half == 0:
                    pe.wait_ge(w_split, len(PIECES) * (2 * p + par) + 2)

                def cols(at):
                    return [(w_hi[par][:, at + kc * P:at + kc * P + P], w_lo[par][:, at + kc * P:at + kc * P + P],
                             c_hi[:, kc, tok_of(half)], c_lo[:, kc, tok_of(half)]) for kc in range(KC)]

                if j < FULL:
                    product(gate_ps[n % 2][:, :], cols(j * ITEM_COLS), True, True).then_inc(gates_done, 1)
                    if before_up:
                        before_up()
                    product(up_ps[n % 2][:, :], cols(j * ITEM_COLS + KC * P), True, True).then_inc(ups_done, 1)
                else:
                    product(gate_ps[n % 2][:, :], cols(TAILS_AT), True, True).then_inc(gates_done, 1)

            def down(n, p, last_pair):
                par, half, j = unit_of(n)
                if not has_down(n):
                    return
                pe.wait_ge(h_lo_ready, ITEMS * p + n + 1)
                if j < FULL:
                    if j == 0 and half == 0:
                        pe.wait_ge(w_split, len(PIECES) * (2 * p + par + 1))
                    at, whi, wlo, hhi, hlo = DOWN_AT + j * DIM, w_hi[par], w_lo[par], h_hi[n % RING], h_lo[n % RING]
                else:
                    if half == 0:
                        pe.wait_ge(wt_split, p + 1)
                    at, whi, wlo, hhi, hlo = 0, wt_hi, wt_lo, t_hi[half], t_lo[half]
                final = last_pair and par == 1 and j == FULL
                for oc in range(KC):
                    cols = slice(at + oc * P, at + oc * P + P)
                    last = product(acc[:, half, oc, :], [(whi[:, cols], wlo[:, cols], hhi[:, :], hlo[:, :])],
                                   False, final)
                    if final and oc == 0:
                        last.then_inc(last_oc_done, 1)
                last.then_inc(downs_done, 1)

            def clear(h):
                for oc in range(KC):
                    nc.tensor.matmul(acc[:, h, oc, :], zeros[:, :], wide_zeros, start=True, stop=False)

            adapters(0)
            base(0)
            low_rank(0)
            adapters(1)
            base(1)
            logits(0)
            low_rank(1)
            gate_up(0, 0)
            logits(1)
            gate_up(1, 0, lambda: pe.wait_ge(logits_read, 1))
            clear(0)
            pe.wait_ge(hid_done, 1)
            gate_up(2, 0)
            pe.wait_ge(consts_ready, 1)
            pe.wait_ge(combine_ready, 1)
            for t in range(TILES // HALVES):
                last = nc.tensor.matmul(acc[:, 1, 0, t * P:(t + 1) * P], comb_et[:, 0, t:t + 1].broadcast_to([P, P]),
                                        ident[:, :], start=True, stop=True)
            last.then_inc(spread_done, 1)
            nc.tensor.matmul(acc[0:EXPERTS * TILES, 1, 1, 0:P], comb_et[:, :, :].rearrange("p e t -> p (e t)"),
                             ident[:, :], start=True, stop=True).then_inc(combT_done, 1)
            pe.wait_ge(hid_done, 2)
            gate_up(3, 0)
            pe.wait_ge(spread_copied, 1)
            pe.wait_ge(combT_copied, 1)
            clear(1)

            def pair(p, last_pair):
                for n in range(ITEMS):
                    ahead = n + LAG
                    if ahead < ITEMS or not last_pair:
                        q = p if ahead < ITEMS else p + 1
                        pe.wait_ge(hid_done, ITEMS * p + ahead - 1)
                        gate_up(ahead % ITEMS, q)
                    down(n, p, last_pair)

            with pe.Fori(0, PAIRS - 1) as p:
                pair(p, False)
            pair(PAIRS - 1, True)


def kernel(**inputs):
    import numpy as np
    import concourse.bacc as bacc
    from concourse.bass_utils import run_bass_kernel_spmd

    def chunked(a):
        return a.reshape(KC, P, *a.shape[1:]).swapaxes(0, 1)

    x = np.asarray(inputs["x"]).reshape(TOKENS, DIM)
    scal = np.repeat(np.asarray(inputs["L0_cond_scalings"]), RANK).reshape(P, 1)
    pack = np.concatenate([
        chunked(np.asarray(inputs["L0_cond_A"]).reshape(ADAPTERS * RANK, DIM).T).reshape(P, KC * P),
        chunked(np.asarray(inputs["L0_cond_W"]).T).reshape(P, KC * DIM),
        np.asarray(inputs["L0_cond_Bm"]).transpose(0, 2, 1).reshape(ADAPTERS * RANK, DIM),
        chunked(np.asarray(inputs["L0_ffn_w_gate"]).T).reshape(P, KC * EXPERTS),
        scal], axis=1)
    w1, w2, w3 = (np.asarray(inputs[f"L0_ffn_w{i}"]) for i in (1, 2, 3))
    body = FULL * P
    gate, up = w1.transpose(0, 2, 1), w3.transpose(0, 2, 1)
    full = np.stack([gate[:, :, :body], up[:, :, :body]])
    full = full.reshape(2, EXPERTS, KC, P, FULL, P).transpose(1, 3, 4, 0, 2, 5).reshape(EXPERTS, P, TAILS_AT)
    tails = np.concatenate([gate[:, :, body:], up[:, :, body:]], axis=2)
    tails = tails.reshape(EXPERTS, KC, P, 2 * TAIL).transpose(0, 2, 1, 3).reshape(EXPERTS, P, KC * 2 * TAIL)
    dn = w2.transpose(0, 2, 1)
    dn_full = dn[:, :body].reshape(EXPERTS, FULL, P, DIM).transpose(0, 2, 1, 3).reshape(EXPERTS, P, FULL * DIM)
    arrays = {
        "x_t": chunked(x.T),
        "small_weights": pack,
        "adapter_of_batch": np.broadcast_to(np.asarray(inputs["itok_B_0_6"]), (P, BATCH)),
        "expert_weights": np.concatenate([full, tails, dn_full], axis=2),
        "tail_down_weights": dn[:, body:].reshape(PAIRS, P, DIM),
    }
    arrays = {k: np.ascontiguousarray(v) for k, v in arrays.items()}

    nc = bacc.Bacc("TRN2", target_bir_lowering=False, num_devices=1)
    args = [nc.dram_tensor(k, v.shape, mybir.dt.from_np(v.dtype), kind="ExternalInput").ap()
            for k, v in arrays.items()]
    comb_dram = nc.dram_tensor("combine_t", (EXPERTS, TOKENS), F32, kind="Internal").ap()
    out = nc.dram_tensor("out_t", (P, KC, TOKENS), F32, kind="ExternalOutput").ap()
    moe_kernel(nc, *args, comb_dram, out)
    got = run_bass_kernel_spmd(nc, [arrays], core_ids=[0]).results[0]["out_t"]
    return got.transpose(1, 0, 2).reshape(DIM, TOKENS).T.reshape(BATCH, SEQ, DIM)
```
